# Optimizing a Trainium2 kernel written in Bass

```python
import numpy as np
import jax
import jax.numpy as jnp

def _softmax(x, axis=-1):
    return jax.nn.softmax(x, axis=axis)

def _gelu(x):
    return jax.nn.gelu(x, approximate=True)

def _silu(x):
    return jax.nn.silu(x)

def _sigmoid(x):
    return jax.nn.sigmoid(x)

def _layernorm(x, axis=-1, eps=1e-05):
    m = jnp.mean(x, axis=axis, keepdims=True)
    v = jnp.var(x, axis=axis, keepdims=True)
    return (x - m) / jnp.sqrt(v + eps)

def _scatter_add(tgt, idx, src, axis=0):
    return tgt.at[idx].add(src)

def _segment_sum(src, seg, n):
    return jax.ops.segment_sum(src, seg, n)
kernel_name = 'mk_dlrm_tower_d1_rec_r8_334c3c'

def setup_inputs(seed: int=0):
    np.random.seed(seed)
    _w = jnp.asarray

    def _rec_inputs():
        import jax
        import jax.numpy as jnp
        _tk = jax.random.key(seed)
        ids = jnp.stack([jax.random.randint(jax.random.fold_in(_tk, 200 + f), (512,), 0, v, jnp.int32) for f, v in enumerate([1000, 1000, 12500, 12500, 12500, 1000, 1000, 12500, 125000, 1000, 1000, 12500, 1250, 1250, 12500, 12500, 12500, 1000, 1000, 12500, 1250, 1250, 1000, 1000, 1000, 1000])], axis=1)
        tbl_0 = 0.05 * jax.random.normal(jax.random.fold_in(_tk, 500 + 0), (1000, 128), jnp.float32)
        tbl_1 = 0.05 * jax.random.normal(jax.random.fold_in(_tk, 500 + 1), (1000, 128), jnp.float32)
        tbl_2 = 0.05 * jax.random.normal(jax.random.fold_in(_tk, 500 + 2), (12500, 128), jnp.float32)
        tbl_3 = 0.05 * jax.random.normal(jax.random.fold_in(_tk, 500 + 3), (12500, 128), jnp.float32)
        tbl_4 = 0.05 * jax.random.normal(jax.random.fold_in(_tk, 500 + 4), (12500, 128), jnp.float32)
        tbl_5 = 0.05 * jax.random.normal(jax.random.fold_in(_tk, 500 + 5), (1000, 128), jnp.float32)
        tbl_6 = 0.05 * jax.random.normal(jax.random.fold_in(_tk, 500 + 6), (1000, 128), jnp.float32)
        tbl_7 = 0.05 * jax.random.normal(jax.random.fold_in(_tk, 500 + 7), (12500, 128), jnp.float32)
        tbl_8 = 0.05 * jax.random.normal(jax.random.fold_in(_tk, 500 + 8), (125000, 128), jnp.float32)
        tbl_9 = 0.05 * jax.random.normal(jax.random.fold_in(_tk, 500 + 9), (1000, 128), jnp.float32)
        tbl_10 = 0.05 * jax.random.normal(jax.random.fold_in(_tk, 500 + 10), (1000, 128), jnp.float32)
        tbl_11 = 0.05 * jax.random.normal(jax.random.fold_in(_tk, 500 + 11), (12500, 128), jnp.float32)
        tbl_12 = 0.05 * jax.random.normal(jax.random.fold_in(_tk, 500 + 12), (1250, 128), jnp.float32)
        tbl_13 = 0.05 * jax.random.normal(jax.random.fold_in(_tk, 500 + 13), (1250, 128), jnp.float32)
        tbl_14 = 0.05 * jax.random.normal(jax.random.fold_in(_tk, 500 + 14), (12500, 128), jnp.float32)
        tbl_15 = 0.05 * jax.random.normal(jax.random.fold_in(_tk, 500 + 15), (12500, 128), jnp.float32)
        tbl_16 = 0.05 * jax.random.normal(jax.random.fold_in(_tk, 500 + 16), (12500, 128), jnp.float32)
        tbl_17 = 0.05 * jax.random.normal(jax.random.fold_in(_tk, 500 + 17), (1000, 128), jnp.float32)
        tbl_18 = 0.05 * jax.random.normal(jax.random.fold_in(_tk, 500 + 18), (1000, 128), jnp.float32)
        tbl_19 = 0.05 * jax.random.normal(jax.random.fold_in(_tk, 500 + 19), (12500, 128), jnp.float32)
        tbl_20 = 0.05 * jax.random.normal(jax.random.fold_in(_tk, 500 + 20), (1250, 128), jnp.float32)
        tbl_21 = 0.05 * jax.random.normal(jax.random.fold_in(_tk, 500 + 21), (1250, 128), jnp.float32)
        tbl_22 = 0.05 * jax.random.normal(jax.random.fold_in(_tk, 500 + 22), (1000, 128), jnp.float32)
        tbl_23 = 0.05 * jax.random.normal(jax.random.fold_in(_tk, 500 + 23), (1000, 128), jnp.float32)
        tbl_24 = 0.05 * jax.random.normal(jax.random.fold_in(_tk, 500 + 24), (1000, 128), jnp.float32)
        tbl_25 = 0.05 * jax.random.normal(jax.random.fold_in(_tk, 500 + 25), (1000, 128), jnp.float32)
        _rk = jax.random.fold_in(_tk, 7)
        r_dense_features = -0.000520686 + 1.00062 * jax.random.normal(jax.random.fold_in(_rk, 101), (512, 128), jnp.float32)
        W_top1 = 0.0405887 * jax.random.normal(jax.random.fold_in(_tk, 801), (607, 512), jnp.float32)
        W_top2 = 0.0441942 * jax.random.normal(jax.random.fold_in(_tk, 802), (512, 256), jnp.float32)
        W_top3 = 0.0625 * jax.random.normal(jax.random.fold_in(_tk, 803), (256, 1), jnp.float32)
        b_top1 = jnp.zeros((512,), jnp.float32)
        b_top2 = jnp.zeros((256,), jnp.float32)
        return (r_dense_features, ids, tbl_0, tbl_1, tbl_2, tbl_3, tbl_4, tbl_5, tbl_6, tbl_7, tbl_8, tbl_9, tbl_10, tbl_11, tbl_12, tbl_13, tbl_14, tbl_15, tbl_16, tbl_17, tbl_18, tbl_19, tbl_20, tbl_21, tbl_22, tbl_23, tbl_24, tbl_25, W_top1, b_top1, W_top2, b_top2, W_top3)
    r_dense_features, ids, tbl_0, tbl_1, tbl_2, tbl_3, tbl_4, tbl_5, tbl_6, tbl_7, tbl_8, tbl_9, tbl_10, tbl_11, tbl_12, tbl_13, tbl_14, tbl_15, tbl_16, tbl_17, tbl_18, tbl_19, tbl_20, tbl_21, tbl_22, tbl_23, tbl_24, tbl_25, W_top1, b_top1, W_top2, b_top2, W_top3 = _rec_inputs()

    def _L0_rec_setup():
        import jax, jax.numpy as jnp
        import numpy as np
        NUM_SPARSE = 26
        EMBED_DIM = 128
        BATCH = 2048
        key = jax.random.key(seed)
        k1, k2 = jax.random.split(key)
        dense_features = jax.random.normal(k1, (BATCH, EMBED_DIM), dtype=jnp.float32)
        sparse_features = jax.random.normal(k2, (BATCH, NUM_SPARSE, EMBED_DIM), dtype=jnp.float32)
        return {'dense_features': dense_features, 'sparse_features': sparse_features}
    _L0_rec_all = _L0_rec_setup()
    _L0_rec_in = {k: v for k, v in _L0_rec_all.items() if k in ()}
    del _L0_rec_all
    return {'r_dense_features': r_dense_features, 'ids': ids, 'tbl_0': tbl_0, 'tbl_1': tbl_1, 'tbl_2': tbl_2, 'tbl_3': tbl_3, 'tbl_4': tbl_4, 'tbl_5': tbl_5, 'tbl_6': tbl_6, 'tbl_7': tbl_7, 'tbl_8': tbl_8, 'tbl_9': tbl_9, 'tbl_10': tbl_10, 'tbl_11': tbl_11, 'tbl_12': tbl_12, 'tbl_13': tbl_13, 'tbl_14': tbl_14, 'tbl_15': tbl_15, 'tbl_16': tbl_16, 'tbl_17': tbl_17, 'tbl_18': tbl_18, 'tbl_19': tbl_19, 'tbl_20': tbl_20, 'tbl_21': tbl_21, 'tbl_22': tbl_22, 'tbl_23': tbl_23, 'tbl_24': tbl_24, 'tbl_25': tbl_25, 'W_top1': W_top1, 'b_top1': b_top1, 'W_top2': W_top2, 'b_top2': b_top2, 'W_top3': W_top3}

def reference(r_dense_features, ids, tbl_0, tbl_1, tbl_2, tbl_3, tbl_4, tbl_5, tbl_6, tbl_7, tbl_8, tbl_9, tbl_10, tbl_11, tbl_12, tbl_13, tbl_14, tbl_15, tbl_16, tbl_17, tbl_18, tbl_19, tbl_20, tbl_21, tbl_22, tbl_23, tbl_24, tbl_25, W_top1, b_top1, W_top2, b_top2, W_top3):
    import jax
    import jax.numpy as jnp

    def _L0_rec_ref(dense_features, sparse_features):
        import jax, jax.numpy as jnp
        import numpy as np
        NUM_SPARSE = 26
        EMBED_DIM = 128
        BATCH = 2048
        F = NUM_SPARSE + 1
        combined = jnp.concatenate([dense_features[:, None, :], sparse_features], axis=1)
        interactions = jnp.einsum('bfd,bgd->bfg', combined, combined)
        iu, ju = jnp.triu_indices(F, k=1)
        interactions_flat = interactions[:, iu, ju]
        return jnp.concatenate([dense_features, interactions_flat], axis=1)
    e = jnp.stack([tbl_0[ids[:, 0]], tbl_1[ids[:, 1]], tbl_2[ids[:, 2]], tbl_3[ids[:, 3]], tbl_4[ids[:, 4]], tbl_5[ids[:, 5]], tbl_6[ids[:, 6]], tbl_7[ids[:, 7]], tbl_8[ids[:, 8]], tbl_9[ids[:, 9]], tbl_10[ids[:, 10]], tbl_11[ids[:, 11]], tbl_12[ids[:, 12]], tbl_13[ids[:, 13]], tbl_14[ids[:, 14]], tbl_15[ids[:, 15]], tbl_16[ids[:, 16]], tbl_17[ids[:, 17]], tbl_18[ids[:, 18]], tbl_19[ids[:, 19]], tbl_20[ids[:, 20]], tbl_21[ids[:, 21]], tbl_22[ids[:, 22]], tbl_23[ids[:, 23]], tbl_24[ids[:, 24]], tbl_25[ids[:, 25]]], axis=1)
    z = _L0_rec_ref(r_dense_features, e)
    z = z.reshape(z.shape[0], -1)
    h = jnp.concatenate([z, r_dense_features], axis=1)
    h = jnp.maximum(h @ W_top1 + b_top1, 0.0)
    h = jnp.maximum(h @ W_top2 + b_top2, 0.0)
    y = h @ W_top3
    return y

_drawn_inputs = setup_inputs


def setup_inputs(seed=0):
    import zlib

    import numpy as np

    out = dict(_drawn_inputs(seed))
    spreads = {'b_top1': (0.0, 0.1), 'b_top2': (0.0, 0.1)}
    factors = {}
    for name, (base, spread) in spreads.items():
        noise = np.random.default_rng([zlib.crc32(name.encode()), seed]).standard_normal(out[name].shape)
        drawn = base * np.exp(spread * noise) if base else spread * noise
        out[name] = jnp.asarray(drawn.astype(out[name].dtype))
    for name, factor in factors.items():
        out[name] = (out[name] * factor).astype(out[name].dtype)
    return out
```

```python
from contextlib import ExitStack

import numpy as np

import concourse.bass as bass
from concourse import mybir

F32 = mybir.dt.float32
F32R = mybir.dt.float32r
I32 = mybir.dt.int32
ALU = mybir.AluOpType
ACT = mybir.ActivationFunctionType

P = 128
B, D = 512, 128
TABLES = 26
F = TABLES + 1
TILES = B // P
N1, N2 = 512, 256
C1, C2 = N1 // P, N2 // P

K_PAIR = (F - 1) // 2
F_CHUNK = 9
PAIR_CHUNKS = F // F_CHUNK
PAIR_ROWS = F_CHUNK * K_PAIR
PAIRS = F * (F - 1) // 2
FEATURE_PAD = 32
SQUARE_STRIDE = F + K_PAIR

SAMPLES = 4
GROUP = SAMPLES * F
GROUPS_IN_BANK = 512 // GROUP
UNIT_BANKS = 2
UNIT_GROUPS = GROUPS_IN_BANK * UNIT_BANKS
TILE_GROUPS = P // SAMPLES
GRAM_UNITS = TILE_GROUPS // UNIT_GROUPS

SMALL_ROWS, SMALL_CHUNKS = 1000, 8
SMALL_PARTS = SMALL_ROWS // SMALL_CHUNKS
HOT = 8
SLOTS = 3
ONEHOTS = 8
ROWS_UNIT = 4


def plan(units):
    order = [("dense", 0, 0)]
    early = [("rows", t, q) for t in (0, 1) for q in range(units)]
    for k in range(HOT):
        order.append(("hot", k, 0))
        if k >= 1 and early:
            order.append(early.pop(0))
    order += early
    late = [("rows", t, q) for t in (2, 3) for q in range(units)]
    per = (units + 1) // 2
    order += [("gram", 0, 0)] + late[:per] + [("pairs", 0, 0), ("gram", 1, 0), ("layer1", 0, 0)]
    order += late[per:units] + [("layer2", 0, 0), ("layer3", 0, 0), ("pairs", 1, 0), ("gram", 2, 0)]
    order += [("layer1", 1, 0), ("layer2", 1, 0), ("layer3", 1, 0)]
    order += late[units:units + per] + [("pairs", 2, 0), ("layer1", 2, 0), ("layer2", 2, 0), ("layer3", 2, 0)]
    order += late[units + per:] + [("gram", 3, 0), ("pairs", 3, 0), ("layer1", 3, 0), ("layer2", 3, 0), ("layer3", 3, 0)]
    return order


def build_tower(nc, dense, ids, ids_t, tables, w1, b1, w2, b2, w3, out):
    small = [i for i in range(TABLES) if tables[i].shape[0] == SMALL_ROWS]
    hot = small[:HOT]
    gathered = [i for i in range(TABLES) if i not in hot]
    units = [gathered[i:i + ROWS_UNIT] for i in range(0, len(gathered), ROWS_UNIT)]
    order = plan(len(units))
    feature_unit = {}
    for stage in order:
        if stage[0] in ("dense", "hot", "rows"):
            feature_unit[stage] = len(feature_unit)

    with ExitStack() as ctx:
        def sbuf(name, shape, dtype=F32):
            return ctx.enter_context(nc.sbuf_tensor(name, shape, dtype))

        def psum(name, cols=512):
            return ctx.enter_context(nc.psum_tensor(name, [P, cols], F32))

        def sem(name):
            return ctx.enter_context(nc.semaphore(name))

        index = sbuf("index", [P, TILES, TABLES], I32)
        ident = sbuf("ident", [P, P])
        row_of = sbuf("row_of", [P, SMALL_CHUNKS])
        dense_sb = sbuf("dense_sb", [P, TILES, D])
        rows = sbuf("rows", [P, TILES, len(gathered), D])
        feat = sbuf("feat", [P, TILES, TILE_GROUPS, SAMPLES, FEATURE_PAD])
        dense_t = sbuf("dense_t", [P, B])
        table_raw = sbuf("table_raw", [P, SLOTS, SMALL_CHUNKS * D])
        ids_row = sbuf("ids_row", [P, SLOTS, B], I32)
        table_high = sbuf("table_high", [P, 2, SMALL_CHUNKS * D], F32R)
        table_low = sbuf("table_low", [P, 2, SMALL_CHUNKS * D], F32R)
        onehot = sbuf("onehot", [P, ONEHOTS, B], F32R)
        blocks = sbuf("blocks", [P, 2, F, 32])
        square = sbuf("square", [P, SQUARE_STRIDE * (F + 1)])
        pairs = sbuf("pairs", [P, 2, PAIRS])
        pairs_t = sbuf("pairs_t", [P, 2, PAIR_CHUNKS, P])
        hidden1 = sbuf("hidden1", [P, 2, C1, P])
        hidden2 = sbuf("hidden2", [P, 2, C2, P])
        w1_dense = sbuf("w1_dense", [P, 3, N1])
        w1_pairs = sbuf("w1_pairs", [P, PAIR_CHUNKS, N1])
        w2_sb = sbuf("w2_sb", [P, C1, N2])
        b1_sb = sbuf("b1_sb", [P, C1])
        b2_sb = sbuf("b2_sb", [P, C2])
        w3_sb = sbuf("w3_sb", [P, C2])
        y_sb = sbuf("y_sb", [1, B])

        feat_ps = [psum(f"feat_ps{i}") for i in range(2)]
        gram_ps = [psum(f"gram_ps{i}", 512 * UNIT_BANKS) for i in range(2)]
        act_ps = psum("act_ps")
        dve_ps = psum("dve_ps")
        y_col = PAIR_CHUNKS * P

        ids_in = sem("ids_in")
        dense_in = sem("dense_in")
        table_in = [sem(f"table_in{i}") for i in range(SLOTS)]
        ids_row_in = [sem(f"ids_row_in{i}") for i in range(SLOTS)]
        weights_in = sem("weights_in")
        rows_in = [[sem(f"rows_in{t}_{q}") for q in range(len(units))] for t in range(TILES)]
        ident_zero = sem("ident_zero")
        ident_ready = sem("ident_ready")
        row_of_ready = sem("row_of_ready")
        pad_ready = sem("pad_ready")
        w1_sum_ready = sem("w1_sum_ready")
        high_ready = sem("high_ready")
        low_ready = sem("low_ready")
        onehot_ready = sem("onehot_ready")
        onehot_used = sem("onehot_used")
        feat_ready = sem("feat_ready")
        feat_copied = sem("feat_copied")
        gram_ready = sem("gram_ready")
        gram_by_act = sem("gram_by_act")
        gram_by_dve = sem("gram_by_dve")
        square_turned = sem("square_turned")
        square_ready = sem("square_ready")
        pairs_taken = sem("pairs_taken")
        pairs_ready = sem("pairs_ready")
        pairs_copied = sem("pairs_copied")
        layer1_ready = sem("layer1_ready")
        relu1_by_act = sem("relu1_by_act")
        relu1_by_dve = sem("relu1_by_dve")
        layer2_ready = sem("layer2_ready")
        relu2_by_act = sem("relu2_by_act")
        relu2_by_dve = sem("relu2_by_dve")
        layer3_ready = sem("layer3_ready")
        y_copied = sem("y_copied")
        y_out = sem("y_out")

        block = ctx.enter_context(nc.Block())

        def high_of(k):
            return table_high[0:SMALL_PARTS, k % 2, :]

        def low_of(k):
            return table_low[0:SMALL_PARTS, k % 2, :]

        def hidden1_ps(c):
            half = C1 // 2
            return (act_ps, dve_ps)[c // half][:, P * (c % half):P * (c % half + 1)]

        def hidden2_ps(c):
            return (act_ps[:, 2 * P:3 * P], dve_ps[:, 0:P])[c]

        def feature_slot(f):
            return feat[:, :, :, :, f].rearrange("p t s j -> p t j s")

        def samples_of(bank):
            return bank[:, :].rearrange("p (t j s) -> p t j s", t=TILES, j=SAMPLES)

        def gram_block(v, j):
            banks = gram_ps[v % 2][32 * j:32 * j + 32, :].rearrange("p (n c) -> p n c", n=UNIT_BANKS)
            own = banks[:, :, 0:GROUPS_IN_BANK * GROUP].rearrange("p n (i s g) -> p g n i s", s=SAMPLES, g=F)
            return own[:, :, :, :, j]

        def block_slot(t, q, j):
            dst = blocks[32 * j:32 * j + 32, t % 2, :, UNIT_GROUPS * q:UNIT_GROUPS * (q + 1)]
            return dst.rearrange("p g (n i) -> p g n i", n=UNIT_BANKS)

        @block.sync
        def _(sp):
            sp.dma_start(index[:, :, :], ids.rearrange("(t p) f -> p t f", p=P)).then_inc(ids_in, 16)
            sp.dma_start(dense_sb[:, :, :], dense.rearrange("(t p) d -> p t d", p=P)).then_inc(dense_in, 16)
            for k, i in enumerate(hot):
                if k >= SLOTS:
                    sp.wait_ge(low_ready, k - SLOTS + 1)
                    sp.wait_ge(onehot_ready, SMALL_CHUNKS * (k - SLOTS + 1))
                sp.dma_start(table_raw[0:SMALL_PARTS, k % SLOTS, :],
                             tables[i].rearrange("(p c) d -> p (c d)", c=SMALL_CHUNKS)).then_inc(table_in[k % SLOTS], 16)
                sp.dma_start(ids_row[0:SMALL_PARTS, k % SLOTS, :],
                             ids_t[i:i + 1, :].broadcast_to((SMALL_PARTS, B))).then_inc(ids_row_in[k % SLOTS], 16)
            sp.dma_start(w1_dense[:, 0:2, :], w1[0:2 * D, :].rearrange("(c p) n -> p c n", p=P)).then_inc(weights_in, 16)
            sp.dma_start(w1_pairs[0:PAIR_ROWS, :, :],
                         w1[2 * D:2 * D + PAIRS, :].rearrange("(c p) n -> p c n", p=PAIR_ROWS)).then_inc(weights_in, 16)
            sp.dma_start(w2_sb[:, :, :], w2.rearrange("(c p) n -> p c n", p=P)).then_inc(weights_in, 16)
            sp.dma_start(b1_sb[:, :], b1).then_inc(weights_in, 16)
            sp.dma_start(b2_sb[:, :], b2).then_inc(weights_in, 16)
            sp.dma_start(w3_sb[:, :], w3).then_inc(weights_in, 16)
            sp.wait_ge(y_copied, TILES)
            sp.dma_start(out.rearrange("b o -> o b"), y_sb[:, :]).then_inc(y_out, 16)
            sp.wait_ge(y_out, 16)

        @block.gpsimd
        def _(pool):
            pool.iota(row_of[:, :], pattern=[[1, SMALL_CHUNKS]], base=0, channel_multiplier=SMALL_CHUNKS,
                      allow_small_or_imprecise_dtypes=True).then_inc(row_of_ready, 1)
            pool.memset(ident[:, :], 0.0).then_inc(ident_zero, 1)
            pool.wait_ge(ident_zero, 1)
            pool.affine_select(out=ident[:, :], in_=ident[:, :], compare_op=ALU.not_equal, fill=1.0, base=0,
                               pattern=[[-1, P]], channel_multiplier=1).then_inc(ident_ready, 1)
            pool.wait_ge(ids_in, 16)
            for t in range(TILES):
                for q, unit in enumerate(units):
                    for i in unit:
                        pool.indirect_dma_start(
                            out=rows[:, t, gathered.index(i), :], out_offset=None, in_=tables[i],
                            in_offset=bass.IndirectOffsetOnAxis(ap=index[:, t, i:i + 1], axis=0),
                        ).then_inc(rows_in[t][q], 16)

        @block.tensor
        def _(pe):
            def take_feat_bank(u):
                if u >= 2:
                    pe.wait_ge(feat_copied, u - 1)
                return feat_ps[u % 2]

            for stage in order:
                name, i, q = stage
                t = i
                if name == "dense":
                    pe.wait_ge(dense_in, 16)
                    pe.wait_ge(ident_ready, 1)
                    bank = take_feat_bank(feature_unit[stage])
                    for tile in range(TILES):
                        last = pe.transpose(bank[:, P * tile:P * (tile + 1)], dense_sb[:, tile, :], ident[:, :])
                    last.then_inc(feat_ready, 1)
                elif name == "hot":
                    bank = take_feat_bank(feature_unit[stage])
                    pe.wait_ge(high_ready, i + 1)
                    pe.wait_ge(low_ready, i + 1)
                    for c in range(SMALL_CHUNKS):
                        n = SMALL_CHUNKS * i + c
                        pe.wait_ge(onehot_ready, n + 1)
                        picks = onehot[0:SMALL_PARTS, n % ONEHOTS, :]
                        pe.matmul(bank[:, :], high_of(i)[:, D * c:D * (c + 1)], picks, start=(c == 0), stop=False)
                        last = pe.matmul(bank[:, :], low_of(i)[:, D * c:D * (c + 1)], picks, start=False,
                                         stop=(c == SMALL_CHUNKS - 1))
                        last.then_inc(onehot_used, 1)
                    pe.wait_ge(onehot_used, SMALL_CHUNKS * (i + 1))
                    pe.sem_inc(feat_ready, 1)
                elif name == "rows":
                    bank = take_feat_bank(feature_unit[stage])
                    pe.wait_ge(rows_in[t][q], 16 * len(units[q]))
                    for n, table in enumerate(units[q]):
                        last = pe.transpose(bank[:, P * n:P * (n + 1)], rows[:, t, gathered.index(table), :], ident[:, :])
                    last.then_inc(feat_ready, 1)
                elif name == "gram":
                    done = max(u for s, u in feature_unit.items() if s[0] != "rows" or s[1] <= t)
                    pe.wait_ge(feat_copied, done + 1)
                    pe.wait_ge(pad_ready, 1)
                    for unit in range(GRAM_UNITS):
                        v = GRAM_UNITS * t + unit
                        if v >= 2:
                            pe.wait_ge(gram_by_act, 2 * (v - 1))
                            pe.wait_ge(gram_by_dve, 2 * (v - 1))
                        for n in range(UNIT_GROUPS):
                            s = UNIT_GROUPS * unit + n
                            own = feat[:, t, s, :, :]
                            at = 512 * (n // GROUPS_IN_BANK) + GROUP * (n % GROUPS_IN_BANK)
                            last = pe.matmul(gram_ps[v % 2][:, at:at + GROUP], own.rearrange("p j f -> p (j f)"),
                                             own[:, :, 0:F], start=True, stop=True)
                        last.then_inc(gram_ready, 1)
                elif name == "pairs":
                    pe.wait_ge(pairs_taken, t + 1)
                    if t >= 1:
                        pe.wait_ge(y_copied, t)
                    for c in range(PAIR_CHUNKS):
                        last = pe.transpose(dve_ps[0:PAIR_ROWS, P * c:P * (c + 1)],
                                            pairs[:, t % 2, PAIR_ROWS * c:PAIR_ROWS * (c + 1)], ident[:, :])
                    last.then_inc(pairs_ready, 1)
                elif name == "layer1":
                    pe.wait_ge(weights_in, 6 * 16)
                    pe.wait_ge(w1_sum_ready, 1)
                    pe.wait_ge(pairs_copied, t + 1)
                    if t >= 1:
                        pe.wait_ge(relu2_by_act, t)
                    for c in range(C1):
                        own = hidden1_ps(c)
                        cols = slice(P * c, P * (c + 1))
                        pe.matmul(own, w1_dense[:, 2, cols], dense_t[:, P * t:P * (t + 1)], start=True, stop=False)
                        for m in range(PAIR_CHUNKS):
                            last = pe.matmul(own, w1_pairs[0:PAIR_ROWS, m, cols], pairs_t[0:PAIR_ROWS, t % 2, m, :],
                                             start=False, stop=(m == PAIR_CHUNKS - 1))
                        last.then_inc(layer1_ready, 1)
                elif name == "layer2":
                    pe.wait_ge(relu1_by_act, C1 // 2 * (t + 1))
                    pe.wait_ge(relu1_by_dve, C1 // 2 * (t + 1))
                    for c in range(C2):
                        for m in range(C1):
                            last = pe.matmul(hidden2_ps(c), w2_sb[:, m, P * c:P * (c + 1)],
                                             hidden1[:, t % 2, m, :], start=(m == 0), stop=(m == C1 - 1))
                        last.then_inc(layer2_ready, 1)
                elif name == "layer3":
                    pe.wait_ge(relu2_by_act, t + 1)
                    pe.wait_ge(relu2_by_dve, t + 1)
                    for m in range(C2):
                        last = pe.matmul(dve_ps[0:1, y_col:y_col + P], w3_sb[:, m:m + 1], hidden2[:, t % 2, m, :],
                                         start=(m == 0), stop=(m == C2 - 1))
                    last.then_inc(layer3_ready, 1)

        @block.scalar
        def _(act):
            def round_high(k):
                act.wait_ge(table_in[k % SLOTS], 16 * (k // SLOTS + 1))
                if k >= 2:
                    act.wait_ge(onehot_used, SMALL_CHUNKS * (k - 1))
                act.activation(high_of(k), table_raw[0:SMALL_PARTS, k % SLOTS, :], ACT.Copy).then_inc(high_ready, 1)

            if HOT:
                round_high(0)
            for stage in order:
                name, i, q = stage
                t = i
                if name in ("dense", "hot", "rows"):
                    if name == "hot" and i + 1 < HOT:
                        round_high(i + 1)
                    u = feature_unit[stage]
                    bank = feat_ps[u % 2]
                    act.wait_ge(feat_ready, u + 1)
                    if name == "dense":
                        act.activation(dense_t[:, :], bank[:, :], ACT.Copy)
                        act.activation(feature_slot(0), samples_of(bank), ACT.Copy).then_inc(feat_copied, 1)
                    elif name == "hot":
                        act.activation(feature_slot(hot[i] + 1), samples_of(bank), ACT.Copy).then_inc(feat_copied, 1)
                    else:
                        runs = []
                        for n, table in enumerate(units[q]):
                            if runs and units[q][n - 1] == table - 1:
                                runs[-1][1] += 1
                            else:
                                runs.append([n, 1])
                        for n, count in runs:
                            first = units[q][n] + 1
                            src = bank[:, P * n:P * (n + count)].rearrange("p (f j s) -> p j s f", f=count, j=SAMPLES)
                            dst = feat[:, t, :, :, first:first + count].rearrange("p s j f -> p j s f")
                            last = act.activation(dst, src, ACT.Copy)
                        last.then_inc(feat_copied, 1)
                elif name == "gram":
                    if t >= 2:
                        act.wait_ge(square_turned, t - 1)
                    for unit in range(GRAM_UNITS):
                        v = GRAM_UNITS * t + unit
                        act.wait_ge(gram_ready, v + 1)
                        for j in (2, 3):
                            act.activation(block_slot(t, unit, j), gram_block(v, j), ACT.Copy).then_inc(gram_by_act, 1)
                elif name == "layer1":
                    act.wait_ge(weights_in, 6 * 16)
                    if t >= 2:
                        act.wait_ge(layer2_ready, C2 * (t - 1))
                    act.wait_ge(layer1_ready, C1 * t + C1 // 2)
                    for c in range(C1 // 2):
                        act.activation(hidden1[:, t % 2, c, :], hidden1_ps(c), ACT.Relu,
                                       bias=b1_sb[:, c:c + 1]).then_inc(relu1_by_act, 1)
                elif name == "layer2":
                    if t >= 2:
                        act.wait_ge(layer3_ready, t - 1)
                    act.wait_ge(layer2_ready, C2 * t + 1)
                    act.activation(hidden2[:, t % 2, 0, :], hidden2_ps(0), ACT.Relu,
                                   bias=b2_sb[:, 0:1]).then_inc(relu2_by_act, 1)

        @block.vector
        def _(dve):
            dve.memset(feat[:, :, :, :, F:FEATURE_PAD].rearrange("p t s j f -> p (t s j) f"), 0.0).then_inc(pad_ready, 1)
            for stage in order:
                name, i, q = stage
                t = i
                if name == "hot":
                    dve.wait_ge(table_in[i % SLOTS], 16 * (i // SLOTS + 1))
                    dve.wait_ge(high_ready, i + 1)
                    if i >= 2:
                        dve.wait_ge(onehot_used, SMALL_CHUNKS * (i - 1))
                    dve.tensor_tensor(low_of(i), table_raw[0:SMALL_PARTS, i % SLOTS, :], high_of(i).bitcast(F32),
                                      ALU.subtract).then_inc(low_ready, 1)
                    dve.wait_ge(ids_row_in[i % SLOTS], 16 * (i // SLOTS + 1))
                    if i == 0:
                        dve.wait_ge(row_of_ready, 1)
                    for c in range(SMALL_CHUNKS):
                        n = SMALL_CHUNKS * i + c
                        if n >= ONEHOTS:
                            dve.wait_ge(onehot_used, n - ONEHOTS + 1)
                        dve.tensor_scalar(onehot[0:SMALL_PARTS, n % ONEHOTS, :], ids_row[0:SMALL_PARTS, i % SLOTS, :],
                                          row_of[0:SMALL_PARTS, c:c + 1], None, ALU.is_equal).then_inc(onehot_ready, 1)
                elif name == "gram":
                    for unit in range(GRAM_UNITS):
                        v = GRAM_UNITS * t + unit
                        dve.wait_ge(gram_ready, v + 1)
                        for j in (0, 1):
                            dve.tensor_copy(block_slot(t, unit, j), gram_block(v, j)).then_inc(gram_by_dve, 1)
                    dve.wait_ge(gram_by_act, 2 * GRAM_UNITS * (t + 1))
                    dve.wait_ge(gram_by_dve, 2 * GRAM_UNITS * (t + 1))
                    if t >= 1:
                        dve.wait_ge(pairs_taken, t)
                    own = square[:, 0:F * SQUARE_STRIDE].rearrange("p (g f) -> p g f", g=F)
                    dve.transpose(own[:, :, 0:FEATURE_PAD], blocks[:, t % 2, :, :]).then_inc(square_turned, 1)
                    dve.wait_ge(square_turned, t + 1)
                    dve.tensor_copy(own[:, F - K_PAIR:F, F:F + K_PAIR], own[:, F - K_PAIR:F, 0:K_PAIR])\
                       .then_inc(square_ready, 1)
                    dve.wait_ge(square_ready, t + 1)
                    if t >= 2:
                        dve.wait_ge(pairs_ready, t - 1)
                    diagonals = square[:, 1:1 + F * (SQUARE_STRIDE + 1)].rearrange("p (f x) -> p f x", f=F)
                    dve.tensor_copy(pairs[:, t % 2, :].rearrange("p (f k) -> p f k", f=F), diagonals[:, :, 0:K_PAIR])\
                       .then_inc(pairs_taken, 1)
                    if t == 0:
                        dve.wait_ge(weights_in, 6 * 16)
                        dve.tensor_tensor(w1_dense[:, 2, :], w1_dense[:, 0, :], w1_dense[:, 1, :], ALU.add)\
                           .then_inc(w1_sum_ready, 1)
                elif name == "pairs":
                    dve.wait_ge(pairs_ready, t + 1)
                    if t >= 2:
                        dve.wait_ge(layer1_ready, C1 * (t - 1))
                    dve.tensor_copy(pairs_t[0:PAIR_ROWS, t % 2, :, :],
                                    dve_ps[0:PAIR_ROWS, 0:PAIR_CHUNKS * P].rearrange("p (c b) -> p c b", b=P))\
                       .then_inc(pairs_copied, 1)
                elif name == "layer1":
                    if t >= 2:
                        dve.wait_ge(layer2_ready, C2 * (t - 1))
                    dve.wait_ge(layer1_ready, C1 * (t + 1))
                    for c in range(C1 // 2, C1):
                        dve.tensor_scalar(hidden1[:, t % 2, c, :], hidden1_ps(c), b1_sb[:, c:c + 1],
                                          0.0, ALU.add, ALU.max).then_inc(relu1_by_dve, 1)
                elif name == "layer2":
                    if t >= 2:
                        dve.wait_ge(layer3_ready, t - 1)
                    dve.wait_ge(layer2_ready, C2 * t + 2)
                    dve.tensor_scalar(hidden2[:, t % 2, 1, :], hidden2_ps(1), b2_sb[:, 1:2], 0.0, ALU.add,
                                      ALU.max).then_inc(relu2_by_dve, 1)
                elif name == "layer3":
                    dve.wait_ge(layer3_ready, t + 1)
                    dve.tensor_copy(y_sb[:, P * t:P * (t + 1)], dve_ps[0:1, y_col:y_col + P]).then_inc(y_copied, 1)


def w1_row_order():
    upper = {}
    for f in range(F):
        for g in range(f + 1, F):
            upper[f, g] = D + len(upper)
    order = list(range(D)) + list(range(D + PAIRS, 2 * D + PAIRS))
    for f in range(F):
        for k in range(1, K_PAIR + 1):
            g = (f + k) % F
            order.append(upper[min(f, g), max(f, g)])
    return np.array(order)


def kernel(**inputs):
    import concourse.bacc as bacc
    from concourse.bass_utils import run_bass_kernel_spmd

    nc = bacc.Bacc("TRN2", target_bir_lowering=False, num_devices=1)
    arrays = {}

    def given(name, a):
        a = np.ascontiguousarray(a)
        arrays[name] = a
        return nc.dram_tensor(name, a.shape, mybir.dt.from_np(a.dtype), kind="ExternalInput").ap()

    dense = given("dense", inputs["r_dense_features"])
    ids = given("ids", inputs["ids"])
    ids_t = given("ids_by_table", np.asarray(inputs["ids"]).T)
    tables = [given(f"table_{i}", inputs[f"tbl_{i}"]) for i in range(TABLES)]
    w1 = given("w_top1_by_pair", np.asarray(inputs["W_top1"])[w1_row_order()])
    w2 = given("w_top2", inputs["W_top2"])
    b1 = given("b_top1_columns", np.asarray(inputs["b_top1"]).reshape(C1, P).T)
    b2 = given("b_top2_columns", np.asarray(inputs["b_top2"]).reshape(C2, P).T)
    w3 = given("w_top3_columns", np.asarray(inputs["W_top3"]).reshape(C2, P).T)
    out = nc.dram_tensor("y", (B, 1), F32, kind="ExternalOutput").ap()
    build_tower(nc, dense, ids, ids_t, tables, w1, b1, w2, b2, w3, out)
    result = run_bass_kernel_spmd(nc, [arrays], core_ids=[0])
    return result.results[0]["y"]
```

```python
from contextlib import ExitStack

import numpy as np

import concourse.bass as bass
from concourse import mybir

F32 = mybir.dt.float32
F32R = mybir.dt.float32r
I32 = mybir.dt.int32
ALU = mybir.AluOpType
ACT = mybir.ActivationFunctionType

P = 128
B, D = 512, 128
TABLES = 26
F = TABLES + 1
TILES = B // P
N1, N2 = 512, 256
C1, C2 = N1 // P, N2 // P

K_PAIR = (F - 1) // 2
F_CHUNK = 9
PAIR_CHUNKS = F // F_CHUNK
PAIR_ROWS = F_CHUNK * K_PAIR
PAIRS = F * (F - 1) // 2
FEATURE_PAD = 32
SQUARE_STRIDE = F + K_PAIR

SAMPLES = 4
GROUP = SAMPLES * F
GROUPS_IN_BANK = 512 // GROUP
UNIT_BANKS = 2
UNIT_GROUPS = GROUPS_IN_BANK * UNIT_BANKS
TILE_GROUPS = P // SAMPLES
GRAM_UNITS = TILE_GROUPS // UNIT_GROUPS

SMALL_ROWS, SMALL_CHUNKS = 1000, 8
SMALL_PARTS = SMALL_ROWS // SMALL_CHUNKS
HOT = 8
SLOTS = 3
DVE_CHUNKS = SMALL_CHUNKS - 1
DVE_ONEHOTS = 8
ACT_ONEHOTS = 2
WARM_UP = 10
ROWS_UNIT = 4


def plan(units):
    rows = [[("rows", t, q) for q in range(units)] for t in range(TILES)]
    order = [("dense", 0, 0)]
    early = rows[0] + rows[1]
    for k in range(HOT):
        order.append(("hot", k, 0))
        if k >= 1 and early:
            order.append(early.pop(0))
    order += early
    half = (units + 1) // 2
    order += [("gram", 0, 0)] + rows[2][:half] + [("pairs", 0, 0)]
    for t in range(1, TILES):
        order += [("gram", t, 0), ("layer1", t - 1, 0)]
        if t + 1 < TILES:
            order += rows[t + 1][half if t == 1 else 0:half + 1]
        order += [("layer2", t - 1, 0), ("layer3", t - 1, 0)]
        if t + 1 < TILES:
            order += rows[t + 1][half + 1:]
        order += [("pairs", t, 0)]
    order += [("layer1", TILES - 1, 0), ("layer2", TILES - 1, 0), ("layer3", TILES - 1, 0)]
    return order


def placed_features(hot, gathered):
    return [0] + [1 + i for i in gathered] + [1 + i for i in hot]


def split_tables(rows_of):
    hot = [i for i in range(TABLES) if rows_of[i] == SMALL_ROWS][:HOT]
    return hot, [i for i in range(TABLES) if i not in hot]


def build_tower(nc, dense, ids, ids_t, tables, w1, b1, w2, b2, w3, out):
    hot, gathered = split_tables([a.shape[0] for a in tables])
    units = [gathered[i:i + ROWS_UNIT] for i in range(0, len(gathered), ROWS_UNIT)]
    order = plan(len(units))
    feature_unit = {}
    for stage in order:
        if stage[0] in ("dense", "hot", "rows"):
            feature_unit[stage] = len(feature_unit)

    with ExitStack() as ctx:
        def sbuf(name, shape, dtype=F32):
            return ctx.enter_context(nc.sbuf_tensor(name, shape, dtype))

        def psum(name, cols=512):
            return ctx.enter_context(nc.psum_tensor(name, [P, cols], F32))

        def sem(name):
            return ctx.enter_context(nc.semaphore(name))

        index = sbuf("index", [P, TILES, TABLES], I32)
        ident = sbuf("ident", [P, P])
        row_of = sbuf("row_of", [P, SMALL_CHUNKS])
        minus_row = sbuf("minus_row", [P, 1])
        distance = sbuf("distance", [P, B])
        dense_sb = sbuf("dense_sb", [P, TILES, D])
        rows = sbuf("rows", [P, TILES, len(gathered), D])
        feat = sbuf("feat", [P, TILES, TILE_GROUPS, SAMPLES, FEATURE_PAD])
        dense_t = sbuf("dense_t", [P, B])
        table_raw = sbuf("table_raw", [P, SLOTS, SMALL_CHUNKS * D])
        ids_row = sbuf("ids_row", [P, SLOTS, B], I32)
        table_high = sbuf("table_high", [P, 2, SMALL_CHUNKS * D], F32R)
        table_low = sbuf("table_low", [P, 2, SMALL_CHUNKS * D], F32R)
        onehot = sbuf("onehot", [P, DVE_ONEHOTS + ACT_ONEHOTS, B], F32R)
        blocks = sbuf("blocks", [P, 2, F, 32])
        square = sbuf("square", [P, SQUARE_STRIDE * (F + 1)])
        pairs = sbuf("pairs", [P, 2, PAIRS])
        pairs_t = sbuf("pairs_t", [P, 2, PAIR_CHUNKS, P])
        hidden1 = sbuf("hidden1", [P, 2, C1, P])
        hidden2 = sbuf("hidden2", [P, 2, C2, P])
        w1_dense = sbuf("w1_dense", [P, 3, N1])
        w1_pairs = sbuf("w1_pairs", [P, PAIR_CHUNKS, N1])
        w2_sb = sbuf("w2_sb", [P, C1, N2])
        b1_sb = sbuf("b1_sb", [P, C1])
        b2_sb = sbuf("b2_sb", [P, C2])
        w3_sb = sbuf("w3_sb", [P, C2])
        y_sb = sbuf("y_sb", [1, B])

        feat_ps = [psum(f"feat_ps{i}") for i in range(2)]
        gram_ps = [psum(f"gram_ps{i}", 512 * UNIT_BANKS) for i in range(2)]
        act_ps = psum("act_ps")
        dve_ps = psum("dve_ps")
        y_col = PAIR_CHUNKS * P

        ids_in = sem("ids_in")
        dense_in = sem("dense_in")
        table_in = [sem(f"table_in{i}") for i in range(SLOTS)]
        ids_row_in = [sem(f"ids_row_in{i}") for i in range(SLOTS)]
        weights_in = sem("weights_in")
        rows_in = [[sem(f"rows_in{t}_{q}") for q in range(len(units))] for t in range(TILES)]
        ident_zero = sem("ident_zero")
        ident_ready = sem("ident_ready")
        row_of_ready = sem("row_of_ready")
        minus_row_ready = sem("minus_row_ready")
        pad_ready = sem("pad_ready")
        w1_sum_ready = sem("w1_sum_ready")
        high_ready = sem("high_ready")
        low_ready = sem("low_ready")
        onehot_by_dve = sem("onehot_by_dve")
        distance_ready = sem("distance_ready")
        onehot_by_act = sem("onehot_by_act")
        onehot_used = sem("onehot_used")
        feat_ready = sem("feat_ready")
        feat_copied = sem("feat_copied")
        gram_ready = sem("gram_ready")
        gram_by_act = sem("gram_by_act")
        gram_by_dve = sem("gram_by_dve")
        square_turned = sem("square_turned")
        square_ready = sem("square_ready")
        pairs_taken = sem("pairs_taken")
        pairs_ready = sem("pairs_ready")
        pairs_copied = sem("pairs_copied")
        layer1_ready = sem("layer1_ready")
        relu1_by_act = sem("relu1_by_act")
        relu1_by_dve = sem("relu1_by_dve")
        layer2_ready = sem("layer2_ready")
        relu2_by_act = sem("relu2_by_act")
        relu2_by_dve = sem("relu2_by_dve")
        layer3_ready = sem("layer3_ready")
        y_copied = sem("y_copied")
        y_out = sem("y_out")

        block = ctx.enter_context(nc.Block())

        def onehot_of(k, c):
            if c < DVE_CHUNKS:
                slot = (DVE_CHUNKS * k + c) % DVE_ONEHOTS
            else:
                slot = DVE_ONEHOTS + k % ACT_ONEHOTS
            return onehot[0:SMALL_PARTS, slot, :]

        def high_of(k):
            return table_high[0:SMALL_PARTS, k % 2, :]

        def low_of(k):
            return table_low[0:SMALL_PARTS, k % 2, :]

        def hidden1_ps(c):
            half = C1 // 2
            return (act_ps, dve_ps)[c // half][:, P * (c % half):P * (c % half + 1)]

        def hidden2_ps(c):
            return (act_ps[:, 2 * P:3 * P], dve_ps[:, 0:P])[c]

        def feature_slot(f):
            return feat[:, :, :, :, f].rearrange("p t s j -> p t j s")

        def samples_of(bank):
            return bank[:, :].rearrange("p (t j s) -> p t j s", t=TILES, j=SAMPLES)

        def gram_block(v, j):
            banks = gram_ps[v % 2][32 * j:32 * j + 32, :].rearrange("p (n c) -> p n c", n=UNIT_BANKS)
            own = banks[:, :, 0:GROUPS_IN_BANK * GROUP].rearrange("p n (i s g) -> p g n i s", s=SAMPLES, g=F)
            return own[:, :, :, :, j]

        def block_slot(t, q, j):
            dst = blocks[32 * j:32 * j + 32, t % 2, :, UNIT_GROUPS * q:UNIT_GROUPS * (q + 1)]
            return dst.rearrange("p g (n i) -> p g n i", n=UNIT_BANKS)

        @block.sync
        def _(sp):
            sp.dma_start(index[:, :, :], ids.rearrange("(t p) f -> p t f", p=P)).then_inc(ids_in, 16)
            for k, i in enumerate(hot):
                if k >= SLOTS:
                    sp.wait_ge(low_ready, k - SLOTS + 1)
                    sp.wait_ge(onehot_by_dve, DVE_CHUNKS * (k - SLOTS + 1))
                    sp.wait_ge(onehot_by_act, k - SLOTS + 1)
                sp.dma_start(ids_row[0:SMALL_PARTS, k % SLOTS, :],
                             ids_t[i:i + 1, :].broadcast_to((SMALL_PARTS, B))).then_inc(ids_row_in[k % SLOTS], 16)
                sp.dma_start(table_raw[0:SMALL_PARTS, k % SLOTS, :],
                             tables[i].rearrange("(p c) d -> p (c d)", c=SMALL_CHUNKS)).then_inc(table_in[k % SLOTS], 16)
                if k == 0:
                    sp.dma_start(dense_sb[:, :, :], dense.rearrange("(t p) d -> p t d", p=P)).then_inc(dense_in, 16)
            sp.dma_start(w1_dense[:, 0:2, :], w1[0:2 * D, :].rearrange("(c p) n -> p c n", p=P)).then_inc(weights_in, 16)
            sp.dma_start(w1_pairs[0:PAIR_ROWS, :, :],
                         w1[2 * D:2 * D + PAIRS, :].rearrange("(c p) n -> p c n", p=PAIR_ROWS)).then_inc(weights_in, 16)
            sp.dma_start(w2_sb[:, :, :], w2.rearrange("(c p) n -> p c n", p=P)).then_inc(weights_in, 16)
            sp.dma_start(b1_sb[:, :], b1).then_inc(weights_in, 16)
            sp.dma_start(b2_sb[:, :], b2).then_inc(weights_in, 16)
            sp.dma_start(w3_sb[:, :], w3).then_inc(weights_in, 16)
            sp.wait_ge(y_copied, TILES)
            sp.dma_start(out.rearrange("b o -> o b"), y_sb[:, :]).then_inc(y_out, 16)
            sp.wait_ge(y_out, 16)

        @block.gpsimd
        def _(pool):
            pool.iota(row_of[:, :], pattern=[[1, SMALL_CHUNKS]], base=0, channel_multiplier=SMALL_CHUNKS,
                      allow_small_or_imprecise_dtypes=True).then_inc(row_of_ready, 1)
            pool.iota(minus_row[:, :], pattern=[[1, 1]], base=-DVE_CHUNKS, channel_multiplier=-SMALL_CHUNKS,
                      allow_small_or_imprecise_dtypes=True).then_inc(minus_row_ready, 1)
            pool.memset(ident[:, :], 0.0).then_inc(ident_zero, 1)
            pool.wait_ge(ident_zero, 1)
            pool.affine_select(out=ident[:, :], in_=ident[:, :], compare_op=ALU.not_equal, fill=1.0, base=0,
                               pattern=[[-1, P]], channel_multiplier=1).then_inc(ident_ready, 1)
            pool.wait_ge(ids_in, 16)
            for t in range(TILES):
                for q, unit in enumerate(units):
                    for i in unit:
                        pool.indirect_dma_start(
                            out=rows[:, t, gathered.index(i), :], out_offset=None, in_=tables[i],
                            in_offset=bass.IndirectOffsetOnAxis(ap=index[:, t, i:i + 1], axis=0),
                        ).then_inc(rows_in[t][q], 16)

        @block.tensor
        def _(pe):
            def take_feat_bank(u):
                if u >= 2:
                    pe.wait_ge(feat_copied, u - 1)
                return feat_ps[u % 2]

            pe.wait_ge(ident_ready, 1)
            for _ in range(WARM_UP):
                pe.matmul(feat_ps[0][:, 0:P], ident[:, :], ident[:, :], start=True, stop=True)

            for stage in order:
                name, i, q = stage
                t = i
                if name == "dense":
                    pe.wait_ge(dense_in, 16)
                    bank = take_feat_bank(feature_unit[stage])
                    for tile in range(TILES):
                        last = pe.transpose(bank[:, P * tile:P * (tile + 1)], dense_sb[:, tile, :], ident[:, :])
                    last.then_inc(feat_ready, 1)
                elif name == "hot":
                    bank = take_feat_bank(feature_unit[stage])
                    pe.wait_ge(high_ready, i + 1)

                    def wait_onehot(c):
                        if c < DVE_CHUNKS:
                            pe.wait_ge(onehot_by_dve, DVE_CHUNKS * i + c + 1)
                        else:
                            pe.wait_ge(onehot_by_act, i + 1)

                    def product(part, c):
                        return pe.matmul(bank[:, :], part[:, D * c:D * (c + 1)], onehot_of(i, c),
                                         start=(c == 0 and part is high), stop=(c == SMALL_CHUNKS - 1 and part is low))

                    high, low = high_of(i), low_of(i)
                    if i == 0:
                        for c in range(SMALL_CHUNKS):
                            wait_onehot(c)
                            product(high, c)
                        pe.wait_ge(low_ready, 1)
                        for c in range(SMALL_CHUNKS):
                            product(low, c).then_inc(onehot_used, 1)
                    else:
                        pe.wait_ge(low_ready, i + 1)
                        for c in range(SMALL_CHUNKS):
                            wait_onehot(c)
                            product(high, c)
                            product(low, c).then_inc(onehot_used, 1)
                    pe.wait_ge(onehot_used, SMALL_CHUNKS * (i + 1))
                    pe.sem_inc(feat_ready, 1)
                elif name == "rows":
                    bank = take_feat_bank(feature_unit[stage])
                    pe.wait_ge(rows_in[t][q], 16 * len(units[q]))
                    for n, table in enumerate(units[q]):
                        last = pe.transpose(bank[:, P * n:P * (n + 1)], rows[:, t, gathered.index(table), :], ident[:, :])
                    last.then_inc(feat_ready, 1)
                elif name == "gram":
                    done = max(u for s, u in feature_unit.items() if s[0] != "rows" or s[1] <= t)
                    pe.wait_ge(feat_copied, done + 1)
                    pe.wait_ge(pad_ready, 1)
                    for unit in range(GRAM_UNITS):
                        v = GRAM_UNITS * t + unit
                        if v >= 2:
                            pe.wait_ge(gram_by_act, 2 * (v - 1))
                            pe.wait_ge(gram_by_dve, 2 * (v - 1))
                        for n in range(UNIT_GROUPS):
                            s = UNIT_GROUPS * unit + n
                            own = feat[:, t, s, :, :]
                            at = 512 * (n // GROUPS_IN_BANK) + GROUP * (n % GROUPS_IN_BANK)
                            last = pe.matmul(gram_ps[v % 2][:, at:at + GROUP], own.rearrange("p j f -> p (j f)"),
                                             own[:, :, 0:F], start=True, stop=True)
                        last.then_inc(gram_ready, 1)
                elif name == "pairs":
                    pe.wait_ge(pairs_taken, t + 1)
                    if t >= 1:
                        pe.wait_ge(y_copied, t)
                    for c in range(PAIR_CHUNKS):
                        last = pe.transpose(dve_ps[0:PAIR_ROWS, P * c:P * (c + 1)],
                                            pairs[:, t % 2, PAIR_ROWS * c:PAIR_ROWS * (c + 1)], ident[:, :])
                    last.then_inc(pairs_ready, 1)
                elif name == "layer1":
                    pe.wait_ge(weights_in, 6 * 16)
                    pe.wait_ge(w1_sum_ready, 1)
                    pe.wait_ge(pairs_copied, t + 1)
                    if t >= 1:
                        pe.wait_ge(relu2_by_act, t)
                    for c in range(C1):
                        own = hidden1_ps(c)
                        cols = slice(P * c, P * (c + 1))
                        pe.matmul(own, w1_dense[:, 2, cols], dense_t[:, P * t:P * (t + 1)], start=True, stop=False)
                        for m in range(PAIR_CHUNKS):
                            last = pe.matmul(own, w1_pairs[0:PAIR_ROWS, m, cols], pairs_t[0:PAIR_ROWS, t % 2, m, :],
                                             start=False, stop=(m == PAIR_CHUNKS - 1))
                        last.then_inc(layer1_ready, 1)
                elif name == "layer2":
                    for c in range(C2):
                        for m in range(C1):
                            if c == 0 and m == 0:
                                pe.wait_ge(relu1_by_act, C1 // 2 * (t + 1))
                            if c == 0 and m == C1 // 2:
                                pe.wait_ge(relu1_by_dve, C1 // 2 * (t + 1))
                            last = pe.matmul(hidden2_ps(c), w2_sb[:, m, P * c:P * (c + 1)],
                                             hidden1[:, t % 2, m, :], start=(m == 0), stop=(m == C1 - 1))
                        last.then_inc(layer2_ready, 1)
                elif name == "layer3":
                    pe.wait_ge(relu2_by_act, t + 1)
                    pe.wait_ge(relu2_by_dve, t + 1)
                    for m in range(C2):
                        last = pe.matmul(dve_ps[0:1, y_col:y_col + P], w3_sb[:, m:m + 1], hidden2[:, t % 2, m, :],
                                         start=(m == 0), stop=(m == C2 - 1))
                    last.then_inc(layer3_ready, 1)

        @block.scalar
        def _(act):
            def round_high(k):
                act.wait_ge(table_in[k % SLOTS], 16 * (k // SLOTS + 1))
                if k >= 2:
                    act.wait_ge(onehot_used, SMALL_CHUNKS * (k - 1))
                act.activation(high_of(k), table_raw[0:SMALL_PARTS, k % SLOTS, :], ACT.Copy).then_inc(high_ready, 1)

            def last_onehot(k):
                if k == 0:
                    act.wait_ge(minus_row_ready, 1)
                if k >= 1:
                    act.wait_ge(onehot_by_act, k)
                act.wait_ge(ids_row_in[k % SLOTS], 16 * (k // SLOTS + 1))
                act.activation(distance[0:SMALL_PARTS, :], ids_row[0:SMALL_PARTS, k % SLOTS, :], ACT.Abs,
                               bias=minus_row[0:SMALL_PARTS, :]).then_inc(distance_ready, 1)
                act.wait_ge(distance_ready, k + 1)
                if k >= ACT_ONEHOTS:
                    act.wait_ge(onehot_used, SMALL_CHUNKS * (k - ACT_ONEHOTS + 1))
                act.activation(onehot_of(k, DVE_CHUNKS), distance[0:SMALL_PARTS, :], ACT.Relu,
                               bias=1.0, scale=-1.0).then_inc(onehot_by_act, 1)

            round_high(0)
            last_onehot(0)
            for stage in order:
                name, i, q = stage
                t = i
                if name in ("dense", "hot", "rows"):
                    if name == "hot" and i + 1 < HOT:
                        round_high(i + 1)
                        last_onehot(i + 1)
                    u = feature_unit[stage]
                    bank = feat_ps[u % 2]
                    act.wait_ge(feat_ready, u + 1)
                    if name == "dense":
                        act.activation(dense_t[:, :], bank[:, :], ACT.Copy)
                        act.activation(feature_slot(0), samples_of(bank), ACT.Copy).then_inc(feat_copied, 1)
                    elif name == "hot":
                        act.activation(feature_slot(1 + len(gathered) + i), samples_of(bank), ACT.Copy).then_inc(feat_copied, 1)
                    else:
                        first, count = 1 + ROWS_UNIT * q, len(units[q])
                        src = bank[:, 0:P * count].rearrange("p (f j s) -> p j s f", f=count, j=SAMPLES)
                        dst = feat[:, t, :, :, first:first + count].rearrange("p s j f -> p j s f")
                        act.activation(dst, src, ACT.Copy).then_inc(feat_copied, 1)
                elif name == "gram":
                    if t >= 2:
                        act.wait_ge(square_turned, t - 1)
                    for unit in range(GRAM_UNITS):
                        v = GRAM_UNITS * t + unit
                        act.wait_ge(gram_ready, v + 1)
                        for j in (2, 3):
                            act.activation(block_slot(t, unit, j), gram_block(v, j), ACT.Copy).then_inc(gram_by_act, 1)
                elif name == "layer1":
                    act.wait_ge(weights_in, 6 * 16)
                    if t >= 2:
                        act.wait_ge(layer2_ready, C2 * (t - 1))
                    act.wait_ge(layer1_ready, C1 * t + C1 // 2)
                    for c in range(C1 // 2):
                        act.activation(hidden1[:, t % 2, c, :], hidden1_ps(c), ACT.Relu,
                                       bias=b1_sb[:, c:c + 1]).then_inc(relu1_by_act, 1)
                elif name == "layer2":
                    if t >= 2:
                        act.wait_ge(layer3_ready, t - 1)
                    act.wait_ge(layer2_ready, C2 * t + 1)
                    act.activation(hidden2[:, t % 2, 0, :], hidden2_ps(0), ACT.Relu,
                                   bias=b2_sb[:, 0:1]).then_inc(relu2_by_act, 1)

        @block.vector
        def _(dve):
            dve.memset(feat[:, :, :, :, F:FEATURE_PAD].rearrange("p t s j f -> p (t s j) f"), 0.0).then_inc(pad_ready, 1)
            for stage in order:
                name, i, q = stage
                t = i
                if name == "hot":
                    def subtract_high():
                        dve.wait_ge(table_in[i % SLOTS], 16 * (i // SLOTS + 1))
                        dve.wait_ge(high_ready, i + 1)
                        if i >= 2:
                            dve.wait_ge(onehot_used, SMALL_CHUNKS * (i - 1))
                        dve.tensor_tensor(low_of(i), table_raw[0:SMALL_PARTS, i % SLOTS, :], high_of(i).bitcast(F32),
                                          ALU.subtract).then_inc(low_ready, 1)

                    if i == 0:
                        dve.wait_ge(row_of_ready, 1)
                    else:
                        subtract_high()
                    dve.wait_ge(ids_row_in[i % SLOTS], 16 * (i // SLOTS + 1))
                    for c in range(DVE_CHUNKS):
                        old = DVE_CHUNKS * i + c - DVE_ONEHOTS
                        if old >= 0:
                            dve.wait_ge(onehot_used, SMALL_CHUNKS * (old // DVE_CHUNKS) + old % DVE_CHUNKS + 1)
                        dve.tensor_scalar(onehot_of(i, c), ids_row[0:SMALL_PARTS, i % SLOTS, :],
                                          row_of[0:SMALL_PARTS, c:c + 1], None, ALU.is_equal).then_inc(onehot_by_dve, 1)
                    if i == 0:
                        subtract_high()
                elif name == "gram":
                    for unit in range(GRAM_UNITS):
                        v = GRAM_UNITS * t + unit
                        dve.wait_ge(gram_ready, v + 1)
                        for j in (0, 1):
                            dve.tensor_copy(block_slot(t, unit, j), gram_block(v, j)).then_inc(gram_by_dve, 1)
                    dve.wait_ge(gram_by_act, 2 * GRAM_UNITS * (t + 1))
                    dve.wait_ge(gram_by_dve, 2 * GRAM_UNITS * (t + 1))
                    if t >= 1:
                        dve.wait_ge(pairs_taken, t)
                    own = square[:, 0:F * SQUARE_STRIDE].rearrange("p (g f) -> p g f", g=F)
                    dve.transpose(own[:, :, 0:FEATURE_PAD], blocks[:, t % 2, :, :]).then_inc(square_turned, 1)
                    dve.wait_ge(square_turned, t + 1)
                    dve.tensor_copy(own[:, F - K_PAIR:F, F:F + K_PAIR], own[:, F - K_PAIR:F, 0:K_PAIR])\
                       .then_inc(square_ready, 1)
                    dve.wait_ge(square_ready, t + 1)
                    if t >= 2:
                        dve.wait_ge(pairs_ready, t - 1)
                    diagonals = square[:, 1:1 + F * (SQUARE_STRIDE + 1)].rearrange("p (f x) -> p f x", f=F)
                    dve.tensor_copy(pairs[:, t % 2, :].rearrange("p (f k) -> p f k", f=F), diagonals[:, :, 0:K_PAIR])\
                       .then_inc(pairs_taken, 1)
                    if t == 0:
                        dve.wait_ge(weights_in, 6 * 16)
                        dve.tensor_tensor(w1_dense[:, 2, :], w1_dense[:, 0, :], w1_dense[:, 1, :], ALU.add)\
                           .then_inc(w1_sum_ready, 1)
                elif name == "pairs":
                    dve.wait_ge(pairs_ready, t + 1)
                    if t >= 2:
                        dve.wait_ge(layer1_ready, C1 * (t - 1))
                    dve.tensor_copy(pairs_t[0:PAIR_ROWS, t % 2, :, :],
                                    dve_ps[0:PAIR_ROWS, 0:PAIR_CHUNKS * P].rearrange("p (c b) -> p c b", b=P))\
                       .then_inc(pairs_copied, 1)
                elif name == "layer1":
                    if t >= 2:
                        dve.wait_ge(layer2_ready, C2 * (t - 1))
                    dve.wait_ge(layer1_ready, C1 * (t + 1))
                    for c in range(C1 // 2, C1):
                        dve.tensor_scalar(hidden1[:, t % 2, c, :], hidden1_ps(c), b1_sb[:, c:c + 1],
                                          0.0, ALU.add, ALU.max).then_inc(relu1_by_dve, 1)
                elif name == "layer2":
                    if t >= 2:
                        dve.wait_ge(layer3_ready, t - 1)
                    dve.wait_ge(layer2_ready, C2 * t + 2)
                    dve.tensor_scalar(hidden2[:, t % 2, 1, :], hidden2_ps(1), b2_sb[:, 1:2], 0.0, ALU.add,
                                      ALU.max).then_inc(relu2_by_dve, 1)
                elif name == "layer3":
                    dve.wait_ge(layer3_ready, t + 1)
                    dve.tensor_copy(y_sb[:, P * t:P * (t + 1)], dve_ps[0:1, y_col:y_col + P]).then_inc(y_copied, 1)


def w1_row_order(feature_at):
    upper = {}
    for f in range(F):
        for g in range(f + 1, F):
            upper[f, g] = D + len(upper)
    order = list(range(D)) + list(range(D + PAIRS, 2 * D + PAIRS))
    for f in range(F):
        for k in range(1, K_PAIR + 1):
            a, b = feature_at[f], feature_at[(f + k) % F]
            order.append(upper[min(a, b), max(a, b)])
    return np.array(order)


def kernel(**inputs):
    import concourse.bacc as bacc
    from concourse.bass_utils import run_bass_kernel_spmd

    nc = bacc.Bacc("TRN2", target_bir_lowering=False, num_devices=1)
    arrays = {}

    def given(name, a):
        a = np.ascontiguousarray(a)
        arrays[name] = a
        return nc.dram_tensor(name, a.shape, mybir.dt.from_np(a.dtype), kind="ExternalInput").ap()

    dense = given("dense", inputs["r_dense_features"])
    ids = given("ids", inputs["ids"])
    ids_t = given("ids_by_table", np.asarray(inputs["ids"]).T)
    tables = [given(f"table_{i}", inputs[f"tbl_{i}"]) for i in range(TABLES)]
    feature_at = placed_features(*split_tables([a.shape[0] for a in tables]))
    w1 = given("w_top1_by_pair", np.asarray(inputs["W_top1"])[w1_row_order(feature_at)])
    w2 = given("w_top2", inputs["W_top2"])
    b1 = given("b_top1_columns", np.asarray(inputs["b_top1"]).reshape(C1, P).T)
    b2 = given("b_top2_columns", np.asarray(inputs["b_top2"]).reshape(C2, P).T)
    w3 = given("w_top3_columns", np.asarray(inputs["W_top3"]).reshape(C2, P).T)
    out = nc.dram_tensor("y", (B, 1), F32, kind="ExternalOutput").ap()
    build_tower(nc, dense, ids, ids_t, tables, w1, b1, w2, b2, w3, out)
    result = run_bass_kernel_spmd(nc, [arrays], core_ids=[0])
    return result.results[0]["y"]
```

```python
from contextlib import ExitStack

import numpy as np

import concourse.bass as bass
from concourse import mybir

F32 = mybir.dt.float32
F32R = mybir.dt.float32r
I32 = mybir.dt.int32
ALU = mybir.AluOpType
ACT = mybir.ActivationFunctionType

P = 128
B, D = 512, 128
TABLES = 26
F = TABLES + 1
TILES = B // P
N1, N2 = 512, 256
C1, C2 = N1 // P, N2 // P

K_PAIR = (F - 1) // 2
F_CHUNK = 9
PAIR_CHUNKS = F // F_CHUNK
PAIR_ROWS = F_CHUNK * K_PAIR
PAIRS = F * (F - 1) // 2
FEATURE_PAD = 32
SQUARE_STRIDE = F + K_PAIR

SAMPLES = 4
GROUP = SAMPLES * F
GROUP_COLS = P
TILE_GROUPS = P // SAMPLES
UNIT_COLS = 1024
UNIT_GROUPS = UNIT_COLS // GROUP_COLS
GRAM_UNITS = TILE_GROUPS // UNIT_GROUPS

SMALL_ROWS, SMALL_CHUNKS = 1000, 8
SMALL_PARTS = SMALL_ROWS // SMALL_CHUNKS
HOT = 9
HALF = 1
HALF_FROM = 1
SLOTS = 3
DVE_CHUNKS = SMALL_CHUNKS - 1
DVE_ONEHOTS = 8
ACT_ONEHOTS = 2
WARM_UP = 9
DENSE_AFTER = 3
AHEAD = [DVE_CHUNKS, 2]
ROWS_UNIT = 4


def plan(units):
    order = [
        ("hot", 0, 0), ("hot", 1, 0), ("rows", 0, 0), ("rows", 0, 1), ("hot", 2, 0), ("rows", 0, 2), ("hot", 3, 0),
        ("hot", 4, 0), ("rows", 0, 3), ("hot", 5, 0), ("rows", 0, 4), ("rows", 1, 0), ("dense", 0, 0), ("hot", 6, 0),
        ("hot", 7, 0), ("rows", 1, 1), ("hot", 8, 0), ("rows", 1, 2), ("rows", 1, 3),
        ("gram", 0, 0), ("rows", 1, 4), ("gram", 0, 1), ("gram", 0, 2), ("gram", 0, 3), ("square", 0, 0),
        ("rows", 2, 0),
        ("gram", 1, 0), ("gram", 1, 1), ("pairs", 0, 0), ("rows", 2, 1), ("gram", 1, 2), ("rows", 2, 2),
        ("layer1", 0, 0), ("rows", 2, 3), ("gram", 1, 3), ("rows", 2, 4), ("layer2", 0, 0), ("square", 1, 0),
        ("gram", 2, 0), ("gram", 2, 1), ("pairs", 1, 0), ("gram", 2, 2), ("rows", 3, 0), ("layer3", 0, 0),
        ("gram", 2, 3), ("rows", 3, 1), ("square", 2, 0), ("layer1", 1, 0), ("rows", 3, 2), ("layer2", 1, 0),
        ("rows", 3, 3), ("rows", 3, 4), ("layer3", 1, 0), ("pairs", 2, 0),
        ("gram", 3, 0), ("gram", 3, 1), ("gram", 3, 2), ("gram", 3, 3),
        ("square", 3, 0), ("layer1", 2, 0), ("pairs", 3, 0), ("layer2", 2, 0), ("layer1_act", 3, 0),
        ("layer1_dve", 3, 0), ("layer2", 3, 0), ("layer3", 2, 0), ("layer3", 3, 0),
    ]
    want = [("hot", k, 0) for k in range(HOT)] + [("dense", 0, 0)]
    for t in range(TILES):
        want += [("rows", t, q) for q in range(units[t])] + [("gram", t, q) for q in range(GRAM_UNITS)]
        want += [(name, t, 0) for name in ("square", "pairs", "layer2", "layer3")]
        want += [(name, t, 0) for name in (["layer1"] if t < TILES - 1 else ["layer1_act", "layer1_dve"])]
    assert sorted(order) == sorted(want)
    return order


def placed_features(hot, gathered):
    picked = sorted(range(HOT), key=place_of)
    return [0] + [1 + i for i in gathered] + [1 + hot[k] for k in picked]


def split_tables(rows_of):
    hot = [i for i in range(TABLES) if rows_of[i] == SMALL_ROWS][:HOT]
    return hot, [i for i in range(TABLES) if i not in hot]


def place_of(k):
    return (k + HALF) % HOT


def first_tile(k):
    return HALF_FROM if k >= HOT - HALF else 0


def build_tower(nc, dense_by_d, ids, ids_t, tables, w1, b1, w2, b2, w3, out):
    hot, gathered = split_tables([a.shape[0] for a in tables])
    gathered_for = [gathered + [i for k, i in enumerate(hot) if t < first_tile(k)] for t in range(TILES)]
    units = [[own[n:n + ROWS_UNIT] for n in range(0, len(own), ROWS_UNIT)] for own in gathered_for]
    order = plan([len(own) for own in units])
    turn = {}
    for stage in order:
        if stage[0] in ("rows", "pairs"):
            turn[stage] = len(turn)

    with ExitStack() as ctx:
        def sbuf(name, shape, dtype=F32):
            return ctx.enter_context(nc.sbuf_tensor(name, shape, dtype))

        def psum(name, cols=512):
            return ctx.enter_context(nc.psum_tensor(name, [P, cols], F32))

        def sem(name):
            return ctx.enter_context(nc.semaphore(name))

        index = sbuf("index", [P, TILES, TABLES], I32)
        ident = sbuf("ident", [P, P])
        row_of = sbuf("row_of", [P, SMALL_CHUNKS])
        minus_row = sbuf("minus_row", [P, 1])
        distance = sbuf("distance", [P, B])
        rows = sbuf("rows", [P, TILES, len(gathered) + HALF, D])
        feat = sbuf("feat", [P, TILES, TILE_GROUPS, SAMPLES, FEATURE_PAD])
        dense_t = sbuf("dense_t", [P, B])
        table_raw = sbuf("table_raw", [P, SLOTS, SMALL_CHUNKS * D])
        ids_row = sbuf("ids_row", [P, SLOTS, B], I32)
        table_high = sbuf("table_high", [P, 2, SMALL_CHUNKS * D], F32R)
        table_low = sbuf("table_low", [P, 2, SMALL_CHUNKS * D], F32R)
        onehot = sbuf("onehot", [P, DVE_ONEHOTS + ACT_ONEHOTS, B], F32R)
        blocks = sbuf("blocks", [P, 2, F, 32])
        square = sbuf("square", [P, SQUARE_STRIDE * (F + 1)])
        pairs = sbuf("pairs", [P, 2, PAIRS])
        pairs_t = sbuf("pairs_t", [P, 2, PAIR_CHUNKS, P])
        hidden1 = sbuf("hidden1", [P, 2, C1, P])
        hidden2 = sbuf("hidden2", [P, 2, C2, P])
        w1_dense = sbuf("w1_dense", [P, 2, N1])
        w1_pairs = sbuf("w1_pairs", [P, PAIR_CHUNKS, N1])
        w2_sb = sbuf("w2_sb", [P, C1, N2])
        b1_sb = sbuf("b1_sb", [P, C1])
        b2_sb = sbuf("b2_sb", [P, C2])
        w3_sb = sbuf("w3_sb", [P, C2])
        y_sb = sbuf("y_sb", [1, B])

        feat_ps = [psum(f"feat_ps{i}") for i in range(2)]
        gram_ps = [psum(f"gram_ps{i}", UNIT_COLS) for i in range(2)]
        act_ps = psum("act_ps")
        dve_ps = psum("dve_ps")
        y_col = (C1 // 2 + 1) * P

        def late(t):
            return t >= TILES - 2

        def y_ps(t):
            if late(t):
                return gram_ps[t % 2][0:1, 0:P]
            return dve_ps[0:1, y_col:y_col + P]

        ids_in = sem("ids_in")
        dense_in = sem("dense_in")
        half_in = sem("half_in")
        table_in = [sem(f"table_in{i}") for i in range(SLOTS)]
        ids_row_in = [sem(f"ids_row_in{i}") for i in range(SLOTS)]
        weights_in = sem("weights_in")
        rows_in = [[sem(f"rows_in{t}_{q}") for q in range(len(units[t]))] for t in range(TILES)]
        ident_zero = sem("ident_zero")
        ident_ready = sem("ident_ready")
        row_of_ready = sem("row_of_ready")
        minus_row_ready = sem("minus_row_ready")
        pad_ready = sem("pad_ready")
        w1_sum_ready = sem("w1_sum_ready")
        half_high_ready = sem("half_high_ready")
        half_low_ready = sem("half_low_ready")
        high_ready = sem("high_ready")
        low_ready = sem("low_ready")
        onehot_by_dve = sem("onehot_by_dve")
        distance_ready = sem("distance_ready")
        onehot_by_act = sem("onehot_by_act")
        onehot_used = sem("onehot_used")
        feat_ready = sem("feat_ready")
        feat_copied = sem("feat_copied")
        dense_placed = sem("dense_placed")
        hot_copied = sem("hot_copied")
        gram_ready = sem("gram_ready")
        gram_by_act = sem("gram_by_act")
        gram_by_dve = sem("gram_by_dve")
        square_turned = sem("square_turned")
        square_ready = sem("square_ready")
        pairs_taken = sem("pairs_taken")
        layer1_ready = sem("layer1_ready")
        relu1_by_act = sem("relu1_by_act")
        relu1_by_dve = sem("relu1_by_dve")
        layer2_ready = sem("layer2_ready")
        relu2_by_act = sem("relu2_by_act")
        relu2_by_dve = sem("relu2_by_dve")
        layer3_ready = sem("layer3_ready")
        y_copied = sem("y_copied")
        y_out = sem("y_out")

        block = ctx.enter_context(nc.Block())

        def onehot_of(k, c):
            if c < DVE_CHUNKS:
                slot = (DVE_CHUNKS * k + c) % DVE_ONEHOTS
            else:
                slot = DVE_ONEHOTS + k % ACT_ONEHOTS
            return onehot[0:SMALL_PARTS, slot, P * first_tile(k):B]

        def ids_of(k):
            return ids_row[0:SMALL_PARTS, k % SLOTS, P * first_tile(k):B]

        def distance_of(k):
            return distance[0:SMALL_PARTS, P * first_tile(k):B]

        def half_cols(h):
            cols = SMALL_CHUNKS // 2 * D
            return slice(cols * h, cols * (h + 1))

        def high_of(k):
            return table_high[0:SMALL_PARTS, k % 2, :]

        def low_of(k):
            return table_low[0:SMALL_PARTS, k % 2, :]

        def hidden1_ps(t, c):
            half = C1 // 2
            if late(t) and c == C1 - 1:
                return gram_ps[t % 2][:, UNIT_COLS // 2:UNIT_COLS // 2 + P]
            return (act_ps, dve_ps)[c // half][:, P * (c % half):P * (c % half + 1)]

        def hidden2_ps(c):
            return (act_ps, dve_ps)[c][:, C1 // 2 * P:(C1 // 2 + 1) * P]

        def feature_slot(f, first):
            return feat[:, first:, :, :, f].rearrange("p t s j -> p t j s")

        def samples_of(bank, first):
            return bank[:, P * first:B].rearrange("p (t j s) -> p t j s", t=TILES - first, j=SAMPLES)

        def gram_unit(t, q):
            return GRAM_UNITS * t + q

        def gram_block(t, q, j):
            own = gram_ps[gram_unit(t, q) % 2][32 * j:32 * j + 32, :].rearrange("p (s c) -> p s c", c=GROUP_COLS)
            return own[:, :, F * j:F * (j + 1)].rearrange("p s g -> p g s")

        def block_slot(t, q, j):
            return blocks[32 * j:32 * j + 32, t % 2, :, UNIT_GROUPS * q:UNIT_GROUPS * (q + 1)]

        def wait_features(engine, t):
            engine.wait_ge(dense_placed, 1)
            engine.wait_ge(hot_copied, HOT)
            engine.wait_ge(feat_copied, 1 + max(turn[s] for s in turn if s[:2] == ("rows", t)))
            engine.wait_ge(pad_ready, 1)

        @block.sync
        def _(sp):
            sp.dma_start(index[:, :, :], ids.rearrange("(t p) f -> p t f", p=P)).then_inc(ids_in, 16)
            for k, i in enumerate(hot):
                if k >= SLOTS:
                    sp.wait_ge(low_ready, k - SLOTS + 1)
                    sp.wait_ge(onehot_by_dve, DVE_CHUNKS * (k - SLOTS + 1))
                    sp.wait_ge(onehot_by_act, k - SLOTS + 1)
                samples = slice(P * first_tile(k), B)
                sp.dma_start(ids_of(k), ids_t[i:i + 1, samples].broadcast_to((SMALL_PARTS, B - samples.start)))\
                  .then_inc(ids_row_in[k % SLOTS], 16)
                table = tables[i].rearrange("(p c) d -> p (c d)", c=SMALL_CHUNKS)
                if k == 0:
                    sp.dma_start(table_raw[0:SMALL_PARTS, 0, half_cols(0)], table[:, half_cols(0)])\
                      .then_inc(half_in, 16)
                    sp.dma_start(table_raw[0:SMALL_PARTS, 0, half_cols(1)], table[:, half_cols(1)])\
                      .then_inc(table_in[0], 16)
                else:
                    sp.dma_start(table_raw[0:SMALL_PARTS, k % SLOTS, :], table).then_inc(table_in[k % SLOTS], 16)
                if k == DENSE_AFTER:
                    sp.dma_start(dense_t[:, :], dense_by_d).then_inc(dense_in, 16)
            sp.dma_start(w1_dense[:, 0:2, :], w1[0:2 * D, :].rearrange("(c p) n -> p c n", p=P)).then_inc(weights_in, 16)
            sp.dma_start(w1_pairs[0:PAIR_ROWS, :, :],
                         w1[2 * D:2 * D + PAIRS, :].rearrange("(c p) n -> p c n", p=PAIR_ROWS)).then_inc(weights_in, 16)
            sp.dma_start(w2_sb[:, :, :], w2.rearrange("(c p) n -> p c n", p=P)).then_inc(weights_in, 16)
            sp.dma_start(b1_sb[:, :], b1).then_inc(weights_in, 16)
            sp.dma_start(b2_sb[:, :], b2).then_inc(weights_in, 16)
            sp.dma_start(w3_sb[:, :], w3).then_inc(weights_in, 16)
            sp.wait_ge(y_copied, TILES)
            sp.dma_start(out.rearrange("b o -> o b"), y_sb[:, :]).then_inc(y_out, 16)
            sp.wait_ge(y_out, 16)

        @block.gpsimd
        def _(pool):
            pool.iota(row_of[:, :], pattern=[[1, SMALL_CHUNKS]], base=0, channel_multiplier=SMALL_CHUNKS,
                      allow_small_or_imprecise_dtypes=True).then_inc(row_of_ready, 1)
            pool.iota(minus_row[:, :], pattern=[[1, 1]], base=-DVE_CHUNKS, channel_multiplier=-SMALL_CHUNKS,
                      allow_small_or_imprecise_dtypes=True).then_inc(minus_row_ready, 1)
            pool.memset(ident[:, :], 0.0).then_inc(ident_zero, 1)
            pool.wait_ge(ident_zero, 1)
            pool.affine_select(out=ident[:, :], in_=ident[:, :], compare_op=ALU.not_equal, fill=1.0, base=0,
                               pattern=[[-1, P]], channel_multiplier=1).then_inc(ident_ready, 1)
            pool.wait_ge(ids_in, 16)
            for t in range(TILES):
                for q, unit in enumerate(units[t]):
                    for i in unit:
                        pool.indirect_dma_start(
                            out=rows[:, t, gathered_for[t].index(i), :], out_offset=None, in_=tables[i],
                            in_offset=bass.IndirectOffsetOnAxis(ap=index[:, t, i:i + 1], axis=0),
                        ).then_inc(rows_in[t][q], 16)

        @block.tensor
        def _(pe):
            def take_feat_bank(u):
                if u >= 2:
                    pe.wait_ge(feat_copied, u - 1)
                return feat_ps[u % 2]

            def wait_gram_bank(b):
                v = gram_unit(TILES, 0) - 2 + b
                pe.wait_ge(gram_by_act, 2 * (v + 1))
                pe.wait_ge(gram_by_dve, 2 * (v + 1))

            pe.wait_ge(ident_ready, 1)
            for _ in range(WARM_UP):
                pe.matmul(feat_ps[0][:, 0:P], ident[:, :], ident[:, :], start=True, stop=True)

            for stage in order:
                name, i, q = stage
                t = i
                if name == "hot":
                    bank = gram_ps[i % 2][:, P * first_tile(i):B]
                    if i >= 2:
                        pe.wait_ge(hot_copied, i - 1)
                    if i >= 1:
                        pe.wait_ge(high_ready, i + 1)

                    def wait_onehot(c):
                        if c < DVE_CHUNKS:
                            pe.wait_ge(onehot_by_dve, DVE_CHUNKS * i + c + 1)
                        else:
                            pe.wait_ge(onehot_by_act, i + 1)

                    def product(part, c):
                        return pe.matmul(bank, part[:, D * c:D * (c + 1)], onehot_of(i, c),
                                         start=(c == 0 and part is high), stop=(c == SMALL_CHUNKS - 1 and part is low))

                    high, low = high_of(i), low_of(i)
                    if i == 0:
                        for c in range(SMALL_CHUNKS):
                            if c == 0:
                                pe.wait_ge(half_high_ready, 1)
                            if c == SMALL_CHUNKS // 2:
                                pe.wait_ge(high_ready, 1)
                            wait_onehot(c)
                            product(high, c)
                        for c in range(SMALL_CHUNKS):
                            if c == 0:
                                pe.wait_ge(half_low_ready, 1)
                            if c == SMALL_CHUNKS // 2:
                                pe.wait_ge(low_ready, 1)
                            product(low, c).then_inc(onehot_used, 1)
                    else:
                        pe.wait_ge(low_ready, i + 1)
                        for c in range(SMALL_CHUNKS):
                            wait_onehot(c)
                            product(high, c)
                            product(low, c).then_inc(onehot_used, 1)
                elif name == "rows":
                    bank = take_feat_bank(turn[stage])
                    pe.wait_ge(rows_in[t][q], 16 * len(units[t][q]))
                    for n, table in enumerate(units[t][q]):
                        last = pe.transpose(bank[:, P * n:P * (n + 1)],
                                            rows[:, t, gathered_for[t].index(table), :], ident[:, :])
                    last.then_inc(feat_ready, 1)
                elif name == "gram":
                    if q == 0:
                        wait_features(pe, t)
                    v = gram_unit(t, q)
                    if v >= 2:
                        pe.wait_ge(gram_by_act, 2 * (v - 1))
                        pe.wait_ge(gram_by_dve, 2 * (v - 1))
                    for n in range(UNIT_GROUPS):
                        own, at = feat[:, t, UNIT_GROUPS * q + n, :, :], GROUP_COLS * n
                        last = pe.matmul(gram_ps[v % 2][:, at:at + GROUP], own.rearrange("p j f -> p (j f)"),
                                         own[:, :, 0:F], start=True, stop=True)
                    last.then_inc(gram_ready, 1)
                elif name == "pairs":
                    bank = take_feat_bank(turn[stage])
                    pe.wait_ge(pairs_taken, t + 1)
                    for c in range(PAIR_CHUNKS):
                        last = pe.transpose(bank[0:PAIR_ROWS, P * c:P * (c + 1)],
                                            pairs[:, t % 2, PAIR_ROWS * c:PAIR_ROWS * (c + 1)], ident[:, :])
                    last.then_inc(feat_ready, 1)
                elif name in ("layer1", "layer1_act", "layer1_dve"):
                    pe.wait_ge(weights_in, 6 * 16)
                    pe.wait_ge(w1_sum_ready, 1)
                    pe.wait_ge(feat_copied, turn["pairs", t, 0] + 1)
                    first, end = {"layer1": (0, C1), "layer1_act": (0, C1 // 2), "layer1_dve": (C1 // 2, C1)}[name]
                    for c in range(first, end):
                        if t >= 1 and c == 0:
                            pe.wait_ge(relu2_by_act, t)
                        if c == C1 // 2:
                            if t == TILES - 1:
                                pe.wait_ge(relu2_by_dve, t)
                            elif t >= 1:
                                pe.wait_ge(y_copied, t)
                        if late(t) and c == C1 - 1:
                            wait_gram_bank(t % 2)
                        own = hidden1_ps(t, c)
                        cols = slice(P * c, P * (c + 1))
                        pe.matmul(own, w1_dense[:, 0, cols], dense_t[:, P * t:P * (t + 1)], start=True, stop=False)
                        for m in range(PAIR_CHUNKS):
                            last = pe.matmul(own, w1_pairs[0:PAIR_ROWS, m, cols], pairs_t[0:PAIR_ROWS, t % 2, m, :],
                                             start=False, stop=(m == PAIR_CHUNKS - 1))
                        last.then_inc(layer1_ready, 1)
                elif name == "layer2":
                    for c in range(C2):
                        for m in range(C1):
                            if c == 0 and m == 0:
                                pe.wait_ge(relu1_by_act, C1 // 2 * (t + 1))
                            if c == 0 and m >= C1 // 2:
                                pe.wait_ge(relu1_by_dve, C1 // 2 * t + m - C1 // 2 + 1)
                            last = pe.matmul(hidden2_ps(c), w2_sb[:, m, P * c:P * (c + 1)],
                                             hidden1[:, t % 2, m, :], start=(m == 0), stop=(m == C1 - 1))
                        last.then_inc(layer2_ready, 1)
                elif name == "layer3":
                    if late(t):
                        wait_gram_bank(t % 2)
                    for m in range(C2):
                        if m == 0:
                            pe.wait_ge(relu2_by_act, t + 1)
                        if m == (1 if late(t) else 0):
                            pe.wait_ge(relu2_by_dve, t + 1)
                        last = pe.matmul(y_ps(t), w3_sb[:, m:m + 1], hidden2[:, t % 2, m, :],
                                         start=(m == 0), stop=(m == C2 - 1))
                    last.then_inc(layer3_ready, 1)

        @block.scalar
        def _(act):
            def round_high(k):
                if k == 0:
                    for h, (came, ready) in enumerate([(half_in, half_high_ready), (table_in[0], high_ready)]):
                        act.wait_ge(came, 16)
                        act.activation(high_of(0)[:, half_cols(h)], table_raw[0:SMALL_PARTS, 0, half_cols(h)],
                                       ACT.Copy).then_inc(ready, 1)
                    return
                act.wait_ge(table_in[k % SLOTS], 16 * (k // SLOTS + 1))
                if k >= 2:
                    act.wait_ge(onehot_used, SMALL_CHUNKS * (k - 1))
                act.activation(high_of(k), table_raw[0:SMALL_PARTS, k % SLOTS, :], ACT.Copy).then_inc(high_ready, 1)

            def last_onehot(k):
                if k == 0:
                    act.wait_ge(minus_row_ready, 1)
                if k >= 1:
                    act.wait_ge(onehot_by_act, k)
                act.wait_ge(ids_row_in[k % SLOTS], 16 * (k // SLOTS + 1))
                act.activation(distance_of(k), ids_of(k), ACT.Abs,
                               bias=minus_row[0:SMALL_PARTS, :]).then_inc(distance_ready, 1)
                act.wait_ge(distance_ready, k + 1)
                if k >= ACT_ONEHOTS:
                    act.wait_ge(onehot_used, SMALL_CHUNKS * (k - ACT_ONEHOTS + 1))
                act.activation(onehot_of(k, DVE_CHUNKS), distance_of(k), ACT.Relu,
                               bias=1.0, scale=-1.0).then_inc(onehot_by_act, 1)

            round_high(0)
            last_onehot(0)
            for stage in order:
                name, i, q = stage
                t = i
                if name == "hot":
                    if i == 0:
                        round_high(1)
                        last_onehot(1)
                    act.wait_ge(onehot_used, SMALL_CHUNKS * (i + 1))
                    if i + 2 < HOT:
                        round_high(i + 2)
                        last_onehot(i + 2)
                    act.activation(feature_slot(1 + len(gathered) + place_of(i), first_tile(i)),
                                   samples_of(gram_ps[i % 2], first_tile(i)), ACT.Copy).then_inc(hot_copied, 1)
                elif name == "dense":
                    act.wait_ge(dense_in, 16)
                    act.activation(feature_slot(0, 0), samples_of(dense_t, 0), ACT.Copy).then_inc(dense_placed, 1)
                elif name in ("rows", "pairs"):
                    u = turn[stage]
                    bank = feat_ps[u % 2]
                    act.wait_ge(feat_ready, u + 1)
                    if name == "pairs":
                        if t >= 2:
                            act.wait_ge(layer1_ready, C1 * (t - 1))
                        act.activation(pairs_t[0:PAIR_ROWS, t % 2, :, :],
                                       bank[0:PAIR_ROWS, 0:PAIR_CHUNKS * P].rearrange("p (c b) -> p c b", b=P),
                                       ACT.Copy).then_inc(feat_copied, 1)
                    else:
                        first, count = 1 + ROWS_UNIT * q, len(units[t][q])
                        src = bank[:, 0:P * count].rearrange("p (f j s) -> p j s f", f=count, j=SAMPLES)
                        dst = feat[:, t, :, :, first:first + count].rearrange("p s j f -> p j s f")
                        act.activation(dst, src, ACT.Copy).then_inc(feat_copied, 1)
                elif name == "gram":
                    if q == 0 and t >= 2:
                        act.wait_ge(square_turned, t - 1)
                    act.wait_ge(gram_ready, gram_unit(t, q) + 1)
                    for j in (2, 3):
                        act.activation(block_slot(t, q, j), gram_block(t, q, j), ACT.Copy).then_inc(gram_by_act, 1)
                elif name in ("layer1", "layer1_act"):
                    act.wait_ge(weights_in, 6 * 16)
                    if t >= 2:
                        act.wait_ge(layer2_ready, C2 * (t - 1))
                    act.wait_ge(layer1_ready, C1 * t + C1 // 2)
                    for c in range(C1 // 2):
                        act.activation(hidden1[:, t % 2, c, :], hidden1_ps(t, c), ACT.Relu,
                                       bias=b1_sb[:, c:c + 1]).then_inc(relu1_by_act, 1)
                elif name == "layer2":
                    if t >= 2:
                        act.wait_ge(layer3_ready, t - 1)
                    act.wait_ge(layer2_ready, C2 * t + 1)
                    act.activation(hidden2[:, t % 2, 0, :], hidden2_ps(0), ACT.Relu,
                                   bias=b2_sb[:, 0:1]).then_inc(relu2_by_act, 1)

        @block.vector
        def _(dve):
            dve.memset(feat[:, :, :, :, F:FEATURE_PAD].rearrange("p t s j f -> p (t s j) f"), 0.0).then_inc(pad_ready, 1)
            for stage in order:
                name, i, q = stage
                t = i
                if name == "hot":
                    def subtract_high():
                        if i == 0:
                            for h, (came, rounded, ready) in enumerate([(half_in, half_high_ready, half_low_ready),
                                                                        (table_in[0], high_ready, low_ready)]):
                                dve.wait_ge(came, 16)
                                dve.wait_ge(rounded, 1)
                                dve.tensor_tensor(low_of(0)[:, half_cols(h)],
                                                  table_raw[0:SMALL_PARTS, 0, half_cols(h)],
                                                  high_of(0)[:, half_cols(h)].bitcast(F32),
                                                  ALU.subtract).then_inc(ready, 1)
                            return
                        dve.wait_ge(table_in[i % SLOTS], 16 * (i // SLOTS + 1))
                        dve.wait_ge(high_ready, i + 1)
                        if i >= 2:
                            dve.wait_ge(onehot_used, SMALL_CHUNKS * (i - 1))
                        dve.tensor_tensor(low_of(i), table_raw[0:SMALL_PARTS, i % SLOTS, :], high_of(i).bitcast(F32),
                                          ALU.subtract).then_inc(low_ready, 1)

                    if i == 0:
                        dve.wait_ge(row_of_ready, 1)
                    ahead = AHEAD[i] if i < len(AHEAD) else 0
                    for c in range(DVE_CHUNKS + 1):
                        if c == ahead:
                            subtract_high()
                        if c == DVE_CHUNKS:
                            break
                        if c == 0:
                            dve.wait_ge(ids_row_in[i % SLOTS], 16 * (i // SLOTS + 1))
                        old = DVE_CHUNKS * i + c - DVE_ONEHOTS
                        if old >= 0:
                            dve.wait_ge(onehot_used, SMALL_CHUNKS * (old // DVE_CHUNKS) + old % DVE_CHUNKS + 1)
                        dve.tensor_scalar(onehot_of(i, c), ids_of(i),
                                          row_of[0:SMALL_PARTS, c:c + 1], None, ALU.is_equal).then_inc(onehot_by_dve, 1)
                elif name == "gram":
                    dve.wait_ge(gram_ready, gram_unit(t, q) + 1)
                    for j in (0, 1):
                        dve.tensor_copy(block_slot(t, q, j), gram_block(t, q, j)).then_inc(gram_by_dve, 1)
                elif name == "square":
                    dve.wait_ge(gram_by_act, 2 * gram_unit(t + 1, 0))
                    dve.wait_ge(gram_by_dve, 2 * gram_unit(t + 1, 0))
                    if t >= 1:
                        dve.wait_ge(pairs_taken, t)
                    own = square[:, 0:F * SQUARE_STRIDE].rearrange("p (g f) -> p g f", g=F)
                    dve.transpose(own[:, :, 0:FEATURE_PAD], blocks[:, t % 2, :, :]).then_inc(square_turned, 1)
                    dve.wait_ge(square_turned, t + 1)
                    dve.tensor_copy(own[:, F - K_PAIR:F, F:F + K_PAIR], own[:, F - K_PAIR:F, 0:K_PAIR])\
                       .then_inc(square_ready, 1)
                    dve.wait_ge(square_ready, t + 1)
                    if t >= 2:
                        dve.wait_ge(feat_copied, turn["pairs", t - 2, 0] + 1)
                    diagonals = square[:, 1:1 + F * (SQUARE_STRIDE + 1)].rearrange("p (f x) -> p f x", f=F)
                    dve.tensor_copy(pairs[:, t % 2, :].rearrange("p (f k) -> p f k", f=F), diagonals[:, :, 0:K_PAIR])\
                       .then_inc(pairs_taken, 1)
                    if t == 0:
                        dve.wait_ge(weights_in, 6 * 16)
                        dve.tensor_tensor(w1_dense[:, 0, :], w1_dense[:, 0, :], w1_dense[:, 1, :], ALU.add)\
                           .then_inc(w1_sum_ready, 1)
                elif name in ("layer1", "layer1_dve"):
                    if t >= 2:
                        dve.wait_ge(layer2_ready, C2 * (t - 1))
                    for c in range(C1 // 2, C1):
                        dve.wait_ge(layer1_ready, C1 * t + c + 1 if late(t) else C1 * (t + 1))
                        dve.tensor_scalar(hidden1[:, t % 2, c, :], hidden1_ps(t, c), b1_sb[:, c:c + 1],
                                          0.0, ALU.add, ALU.max).then_inc(relu1_by_dve, 1)
                elif name == "layer2":
                    if t >= 2:
                        dve.wait_ge(layer3_ready, t - 1)
                    dve.wait_ge(layer2_ready, C2 * t + 2)
                    dve.tensor_scalar(hidden2[:, t % 2, 1, :], hidden2_ps(1), b2_sb[:, 1:2], 0.0, ALU.add,
                                      ALU.max).then_inc(relu2_by_dve, 1)
                elif name == "layer3":
                    dve.wait_ge(layer3_ready, t + 1)
                    dve.tensor_copy(y_sb[:, P * t:P * (t + 1)], y_ps(t)).then_inc(y_copied, 1)


def w1_row_order(feature_at):
    upper = {}
    for f in range(F):
        for g in range(f + 1, F):
            upper[f, g] = D + len(upper)
    order = list(range(D)) + list(range(D + PAIRS, 2 * D + PAIRS))
    for f in range(F):
        for k in range(1, K_PAIR + 1):
            a, b = feature_at[f], feature_at[(f + k) % F]
            order.append(upper[min(a, b), max(a, b)])
    return np.array(order)


def kernel(**inputs):
    import concourse.bacc as bacc
    from concourse.bass_utils import run_bass_kernel_spmd

    nc = bacc.Bacc("TRN2", target_bir_lowering=False, num_devices=1)
    arrays = {}

    def given(name, a):
        a = np.ascontiguousarray(a)
        arrays[name] = a
        return nc.dram_tensor(name, a.shape, mybir.dt.from_np(a.dtype), kind="ExternalInput").ap()

    dense_by_d = given("dense_by_d", np.asarray(inputs["r_dense_features"]).T)
    ids = given("ids", inputs["ids"])
    ids_t = given("ids_by_table", np.asarray(inputs["ids"]).T)
    tables = [given(f"table_{i}", inputs[f"tbl_{i}"]) for i in range(TABLES)]
    feature_at = placed_features(*split_tables([a.shape[0] for a in tables]))
    w1 = given("w_top1_by_pair", np.asarray(inputs["W_top1"])[w1_row_order(feature_at)])
    w2 = given("w_top2", inputs["W_top2"])
    b1 = given("b_top1_columns", np.asarray(inputs["b_top1"]).reshape(C1, P).T)
    b2 = given("b_top2_columns", np.asarray(inputs["b_top2"]).reshape(C2, P).T)
    w3 = given("w_top3_columns", np.asarray(inputs["W_top3"]).reshape(C2, P).T)
    out = nc.dram_tensor("y", (B, 1), F32, kind="ExternalOutput").ap()
    build_tower(nc, dense_by_d, ids, ids_t, tables, w1, b1, w2, b2, w3, out)
    result = run_bass_kernel_spmd(nc, [arrays], core_ids=[0])
    return result.results[0]["y"]
```
